# Optimizing a Trainium2 kernel written in Bass

```python
import numpy as np
import jax
import jax.numpy as jnp

def _softmax(x, axis=-1):
    return jax.nn.softmax(x, axis=axis)

def _gelu(x):
    return jax.nn.gelu(x, approximate=True)

def _silu(x):
    return jax.nn.silu(x)

def _sigmoid(x):
    return jax.nn.sigmoid(x)

def _layernorm(x, axis=-1, eps=1e-05):
    m = jnp.mean(x, axis=axis, keepdims=True)
    v = jnp.var(x, axis=axis, keepdims=True)
    return (x - m) / jnp.sqrt(v + eps)

def _scatter_add(tgt, idx, src, axis=0):
    return tgt.at[idx].add(src)

def _segment_sum(src, seg, n):
    return jax.ops.segment_sum(src, seg, n)
kernel_name = 'mk_early_fusion_d2_tok_img256_r4_55ae3b'

def setup_inputs(seed: int=0):
    np.random.seed(seed)
    _w = jnp.asarray

    def _rec_inputs():
        import jax
        import jax.numpy as jnp
        _rk = jax.random.key(seed)
        x = -7.10856e-05 + 0.999911 * jax.random.normal(jax.random.fold_in(_rk, 1), (16, 1, 96, 96), jnp.float32)
        txt = 7.83249e-05 + 0.02 * jax.random.normal(jax.random.fold_in(_rk, 2), (16, 128, 64), jnp.float32)
        return (x, txt)
    x, txt = _rec_inputs()

    def _L0_tok_setup():
        import jax, jax.numpy as jnp
        import numpy as np
        INV_SQRT2 = 0.7071067811865476

        def haar_dwt2(x):
            lo = (x[..., ::2] + x[..., 1::2]) * INV_SQRT2
            hi = (x[..., ::2] - x[..., 1::2]) * INV_SQRT2
            cA = (lo[..., ::2, :] + lo[..., 1::2, :]) * INV_SQRT2
            cH = (lo[..., ::2, :] - lo[..., 1::2, :]) * INV_SQRT2
            cV = (hi[..., ::2, :] + hi[..., 1::2, :]) * INV_SQRT2
            cD = (hi[..., ::2, :] - hi[..., 1::2, :]) * INV_SQRT2
            return (cA, (cH, cV, cD))

        def wavedec2_maps(x, levels):
            a = x
            details = []
            for _ in range(levels):
                a, d = haar_dwt2(a)
                details.append(d)
            maps = [a]
            for d in reversed(details):
                maps.extend(d)
            return maps
        key = jax.random.key(seed)
        k1, k2 = jax.random.split(key)
        B, H, W_img = (64, 256, 256)
        x = jax.random.normal(k1, (B, 1, H, W_img), dtype=jnp.float32)
        n_maps = 1 + 3 * 2
        W = jax.random.normal(k2, (n_maps, 64), dtype=jnp.float32) * (1.0 / np.sqrt(n_maps))
        b = jnp.zeros((64,), dtype=jnp.float32)
        return {'x': x, 'W': W, 'b': b}
    _L0_tok_all = _L0_tok_setup()
    _L0_tok_in = {k: v for k, v in _L0_tok_all.items() if k in ('W', 'b')}
    del _L0_tok_all

    def _L0_attn_setup():
        import jax, jax.numpy as jnp
        import numpy as np
        key = jax.random.key(seed)
        inputs = jax.random.normal(key, (8, 512, 64), dtype=jnp.float32)
        return {'inputs': inputs}
    _L0_attn_all = _L0_attn_setup()
    _L0_attn_in = {k: v for k, v in _L0_attn_all.items() if k in ()}
    del _L0_attn_all

    def _L0_ffn_setup():
        import jax, jax.numpy as jnp
        import numpy as np
        B, S, D = (8, 1024, 64)
        H = 4 * D
        CAPACITY = 0.5
        key = jax.random.key(seed)
        ks = jax.random.split(key, 6)
        x = jax.random.normal(ks[0], (B, S, D), dtype=jnp.float32)
        attention_mask = jnp.zeros((B, 1, 1, S), dtype=jnp.float32)
        wr = jax.random.normal(ks[1], (D, 1), dtype=jnp.float32) * 0.02
        br = jnp.zeros((1,), dtype=jnp.float32)
        w1 = jax.random.normal(ks[2], (D, H), dtype=jnp.float32) * 0.02
        b1 = jnp.zeros((H,), dtype=jnp.float32)
        w2 = jax.random.normal(ks[3], (H, D), dtype=jnp.float32) * 0.02
        b2 = jnp.zeros((D,), dtype=jnp.float32)
        return {'x': x, 'attention_mask': attention_mask, 'wr': wr, 'br': br, 'w1': w1, 'b1': b1, 'w2': w2, 'b2': b2}
    _L0_ffn_all = _L0_ffn_setup()
    _L0_ffn_in = {k: v for k, v in _L0_ffn_all.items() if k in ('attention_mask', 'wr', 'br', 'w1', 'b1', 'w2', 'b2')}
    del _L0_ffn_all

    def _L1_attn_setup():
        import jax, jax.numpy as jnp
        import numpy as np
        import math
        B, T, D_MODEL = (1, 512, 64)
        N_Q, N_KV = (16, 1)
        D_HEAD = D_MODEL // N_KV
        QPG = N_Q // N_KV
        ROPE_BASE = 10000.0
        WINDOW = 128
        EPS = 1.1920929e-07
        NEG = -1e+30

        def _rope(x, base=ROPE_BASE):
            t, d = (x.shape[-2], x.shape[-1])
            freqs = base ** (-2.0 * jnp.arange(d // 2, dtype=jnp.float32) / d)
            theta = jnp.arange(t, dtype=jnp.float32)[:, None] * freqs[None, :]
            cos, sin = (jnp.cos(theta), jnp.sin(theta))
            x1, x2 = (x[..., 0::2], x[..., 1::2])
            r1 = x1 * cos - x2 * sin
            r2 = x1 * sin + x2 * cos
            return jnp.stack([r1, r2], axis=-1).reshape(x.shape)

        def _rmsnorm(x, w):
            return x * jax.lax.rsqrt(jnp.mean(x * x, axis=-1, keepdims=True) + EPS) * w
        key = jax.random.key(seed)
        k0, k1, k2, k3 = jax.random.split(key, 4)
        x = jax.random.normal(k0, (B, T, D_MODEL), dtype=jnp.float32)
        wq = jax.random.normal(k1, (QPG * N_KV * D_HEAD, D_MODEL), dtype=jnp.float32) * 0.02
        wkv = jax.random.normal(k2, (2 * D_HEAD * N_KV, D_MODEL), dtype=jnp.float32) * 0.02
        wo = jax.random.normal(k3, (D_MODEL, D_HEAD * N_Q * N_KV), dtype=jnp.float32) * 0.02
        q_norm_w = jnp.ones((D_HEAD,), dtype=jnp.float32)
        k_norm_w = jnp.ones((D_HEAD,), dtype=jnp.float32)
        return {'x': x, 'wq': wq, 'wkv': wkv, 'wo': wo, 'q_norm_w': q_norm_w, 'k_norm_w': k_norm_w}
    _L1_attn_all = _L1_attn_setup()
    _L1_attn_in = {k: v for k, v in _L1_attn_all.items() if k in ('wq', 'wkv', 'wo', 'q_norm_w', 'k_norm_w')}
    del _L1_attn_all

    def _L1_ffn_setup():
        import jax, jax.numpy as jnp
        import numpy as np
        B, K, D = (128, 16, 64)
        E = 32
        H = int(D * 0.25)
        key = jax.random.key(seed)
        ks = jax.random.split(key, 7)
        d_rs = D ** (-0.5)
        h_rs = H ** (-0.5)
        x = jax.random.normal(ks[0], (B, K, D), dtype=jnp.float32)
        router_w = jax.random.uniform(ks[1], (E, D), jnp.float32, -d_rs, d_rs)
        router_b = jax.random.uniform(ks[2], (E,), jnp.float32, -d_rs, d_rs)
        W1 = jax.random.uniform(ks[3], (E, D, H), jnp.float32, -h_rs, h_rs)
        b1 = jax.random.uniform(ks[4], (E, H), jnp.float32, -h_rs, h_rs)
        W2 = jax.random.uniform(ks[5], (E, H, D), jnp.float32, -d_rs, d_rs)
        b2 = jax.random.uniform(ks[6], (E, D), jnp.float32, -d_rs, d_rs)
        return {'x': x, 'router_w': router_w, 'router_b': router_b, 'W1': W1, 'b1': b1, 'W2': W2, 'b2': b2}
    _L1_ffn_all = _L1_ffn_setup()
    _L1_ffn_in = {k: v for k, v in _L1_ffn_all.items() if k in ('router_w', 'router_b', 'W1', 'b1', 'W2', 'b2')}
    del _L1_ffn_all
    return {'x': x, 'txt': txt, 'L0_tok_W': _L0_tok_in['W'], 'L0_tok_b': _L0_tok_in['b'], 'L0_ffn_attention_mask': _L0_ffn_in['attention_mask'], 'L0_ffn_wr': _L0_ffn_in['wr'], 'L0_ffn_br': _L0_ffn_in['br'], 'L0_ffn_w1': _L0_ffn_in['w1'], 'L0_ffn_b1': _L0_ffn_in['b1'], 'L0_ffn_w2': _L0_ffn_in['w2'], 'L0_ffn_b2': _L0_ffn_in['b2'], 'L1_attn_wq': _L1_attn_in['wq'], 'L1_attn_wkv': _L1_attn_in['wkv'], 'L1_attn_wo': _L1_attn_in['wo'], 'L1_attn_q_norm_w': _L1_attn_in['q_norm_w'], 'L1_attn_k_norm_w': _L1_attn_in['k_norm_w'], 'L1_ffn_router_w': _L1_ffn_in['router_w'], 'L1_ffn_router_b': _L1_ffn_in['router_b'], 'L1_ffn_W1': _L1_ffn_in['W1'], 'L1_ffn_b1': _L1_ffn_in['b1'], 'L1_ffn_W2': _L1_ffn_in['W2'], 'L1_ffn_b2': _L1_ffn_in['b2']}

def reference(x, txt, L0_tok_W, L0_tok_b, L0_ffn_attention_mask, L0_ffn_wr, L0_ffn_br, L0_ffn_w1, L0_ffn_b1, L0_ffn_w2, L0_ffn_b2, L1_attn_wq, L1_attn_wkv, L1_attn_wo, L1_attn_q_norm_w, L1_attn_k_norm_w, L1_ffn_router_w, L1_ffn_router_b, L1_ffn_W1, L1_ffn_b1, L1_ffn_W2, L1_ffn_b2):
    import jax
    import jax.numpy as jnp

    def _L0_tok_ref(x, W, b):
        import jax, jax.numpy as jnp
        import numpy as np
        INV_SQRT2 = 0.7071067811865476

        def haar_dwt2(x):
            lo = (x[..., ::2] + x[..., 1::2]) * INV_SQRT2
            hi = (x[..., ::2] - x[..., 1::2]) * INV_SQRT2
            cA = (lo[..., ::2, :] + lo[..., 1::2, :]) * INV_SQRT2
            cH = (lo[..., ::2, :] - lo[..., 1::2, :]) * INV_SQRT2
            cV = (hi[..., ::2, :] + hi[..., 1::2, :]) * INV_SQRT2
            cD = (hi[..., ::2, :] - hi[..., 1::2, :]) * INV_SQRT2
            return (cA, (cH, cV, cD))

        def wavedec2_maps(x, levels):
            a = x
            details = []
            for _ in range(levels):
                a, d = haar_dwt2(a)
                details.append(d)
            maps = [a]
            for d in reversed(details):
                maps.extend(d)
            return maps
        imgs = x[:, 0]
        B = imgs.shape[0]
        maps = wavedec2_maps(imgs, 2)
        proc = [jax.image.resize(m, (B, 8, 8), method='bilinear') for m in maps]
        feat = jnp.stack(proc, axis=1)
        feat = feat.reshape(B, feat.shape[1], 64).transpose(0, 2, 1)
        return feat @ W + b

    def _L0_attn_ref(inputs):
        import jax, jax.numpy as jnp
        import numpy as np
        d_k = jnp.asarray(inputs.shape[-1], dtype=inputs.dtype)
        scores = jnp.einsum('bnd,bmd->bnm', inputs, inputs) / jnp.sqrt(d_k)
        weights = jax.nn.softmax(scores, axis=-1)
        context = jnp.einsum('bnm,bmd->bnd', weights, inputs)
        return context

    def _L0_ffn_ref(x, attention_mask, wr, br, w1, b1, w2, b2):
        import jax, jax.numpy as jnp
        import numpy as np
        B, S, D = (8, 1024, 64)
        H = 4 * D
        CAPACITY = 0.5
        b, s, d = x.shape
        weights = (jnp.einsum('bsd,do->bso', x, wr) + br)[..., 0]
        k = max(1, int(CAPACITY * s))
        kk = k - 1 if k > 1 else 1
        _, idx = jax.lax.top_k(weights, k)
        sel_idx = idx[:, :kk]
        sel = jnp.take_along_axis(x, sel_idx[:, :, None], axis=1)
        h = jax.nn.gelu(jnp.einsum('bkd,dh->bkh', sel, w1) + b1)
        y = jnp.einsum('bkh,hd->bkd', h, w2) + b2
        w_sel = jnp.take_along_axis(weights, sel_idx, axis=1)
        y = y * w_sel[..., None]
        batch_idx = jnp.arange(b)[:, None]
        processed = jnp.zeros_like(x).at[batch_idx, sel_idx].set(y)
        return processed + x

    def _L1_attn_ref(x, wq, wkv, wo, q_norm_w, k_norm_w):
        import jax, jax.numpy as jnp
        import numpy as np
        import math
        B, T, D_MODEL = (1, 512, 64)
        N_Q, N_KV = (16, 1)
        D_HEAD = D_MODEL // N_KV
        QPG = N_Q // N_KV
        ROPE_BASE = 10000.0
        WINDOW = 128
        EPS = 1.1920929e-07
        NEG = -1e+30

        def _rope(x, base=ROPE_BASE):
            t, d = (x.shape[-2], x.shape[-1])
            freqs = base ** (-2.0 * jnp.arange(d // 2, dtype=jnp.float32) / d)
            theta = jnp.arange(t, dtype=jnp.float32)[:, None] * freqs[None, :]
            cos, sin = (jnp.cos(theta), jnp.sin(theta))
            x1, x2 = (x[..., 0::2], x[..., 1::2])
            r1 = x1 * cos - x2 * sin
            r2 = x1 * sin + x2 * cos
            return jnp.stack([r1, r2], axis=-1).reshape(x.shape)

        def _rmsnorm(x, w):
            return x * jax.lax.rsqrt(jnp.mean(x * x, axis=-1, keepdims=True) + EPS) * w
        Bx, Tx, C = x.shape
        q = x @ wq.T
        kv = x @ wkv.T
        k, v = (kv[..., :N_KV * D_HEAD], kv[..., N_KV * D_HEAD:])
        q = q.reshape(Bx, Tx, QPG, N_KV, D_HEAD).transpose(0, 2, 3, 1, 4)
        k = k.reshape(Bx, Tx, 1, N_KV, D_HEAD).transpose(0, 2, 3, 1, 4)
        v = v.reshape(Bx, Tx, 1, N_KV, D_HEAD).transpose(0, 2, 3, 1, 4)
        q = _rmsnorm(_rope(q), q_norm_w)
        k = _rmsnorm(_rope(k), k_norm_w)
        rows = jnp.arange(Tx)[:, None]
        cols = jnp.arange(Tx)[None, :]
        mask = (cols <= rows) & (rows - cols <= WINDOW)
        scale = 1.0 / math.sqrt(D_HEAD)
        scores = jnp.einsum('bqgtd,bqgsd->bqgts', q, k) * scale
        scores = jnp.where(mask[None, None, None], scores, NEG)
        attn = jax.nn.softmax(scores, axis=-1)
        out = jnp.einsum('bqgts,bqgsd->bqgtd', attn, v)
        out = out.transpose(0, 3, 1, 2, 4).reshape(Bx, Tx, QPG * N_KV * D_HEAD)
        return out @ wo.T

    def _L1_ffn_ref(x, router_w, router_b, W1, b1, W2, b2):
        import jax, jax.numpy as jnp
        import numpy as np
        B, K, D = (128, 16, 64)
        E = 32
        H = int(D * 0.25)
        xf = x.reshape(-1, D)
        logits = xf @ router_w.T + router_b
        idx = jnp.argmax(logits, axis=-1)
        w1t = jnp.take(W1, idx, axis=0)
        h = jnp.einsum('nd,ndh->nh', xf, w1t) + jnp.take(b1, idx, axis=0)
        h = jax.nn.relu(h)
        w2t = jnp.take(W2, idx, axis=0)
        out = jnp.einsum('nh,nhd->nd', h, w2t) + jnp.take(b2, idx, axis=0)
        out = jax.nn.relu(out)
        return out.reshape(x.shape)
    h = _L0_tok_ref(x, L0_tok_W, L0_tok_b)
    h = jnp.concatenate([h, txt], axis=1)
    h = h + _L0_attn_ref(_layernorm(h, axis=-1))
    h = h + _L0_ffn_ref(_layernorm(h, axis=-1), L0_ffn_attention_mask, L0_ffn_wr, L0_ffn_br, L0_ffn_w1, L0_ffn_b1, L0_ffn_w2, L0_ffn_b2)
    h = h + _L1_attn_ref(_layernorm(h, axis=-1), L1_attn_wq, L1_attn_wkv, L1_attn_wo, L1_attn_q_norm_w, L1_attn_k_norm_w)
    h = h + _L1_ffn_ref(_layernorm(h, axis=-1), L1_ffn_router_w, L1_ffn_router_b, L1_ffn_W1, L1_ffn_b1, L1_ffn_W2, L1_ffn_b2)
    return h

_drawn_inputs = setup_inputs


def setup_inputs(seed=0):
    import zlib

    import numpy as np

    out = dict(_drawn_inputs(seed))
    spreads = {'L0_tok_b': (0.0, 0.1),
     'L0_ffn_b1': (0.0, 0.8),
     'L0_ffn_b2': (0.0, 0.665),
     'L1_attn_q_norm_w': (1.0, 0.6),
     'L1_attn_k_norm_w': (1.0, 0.6)}
    factors = {'L0_ffn_wr': 5.699,
     'L0_ffn_w1': 8.0,
     'L0_ffn_w2': 8.0,
     'L1_attn_wq': 18.149,
     'L1_ffn_b1': 5.818,
     'L1_attn_wkv': 3.425,
     'L1_attn_wo': 3.525,
     'L1_ffn_router_b': 2.895,
     'L1_ffn_b2': 4.626}
    for name, (base, spread) in spreads.items():
        noise = np.random.default_rng([zlib.crc32(name.encode()), seed]).standard_normal(out[name].shape)
        drawn = base * np.exp(spread * noise) if base else spread * noise
        out[name] = jnp.asarray(drawn.astype(out[name].dtype))
    for name, factor in factors.items():
        out[name] = (out[name] * factor).astype(out[name].dtype)
    return out
```

```python
from contextlib import ExitStack

import concourse.bass as bass
from concourse import mybir

ALU = mybir.AluOpType
ACT = mybir.ActivationFunctionType
AX_X = mybir.AxisListType.X
F32 = mybir.dt.float32
F32R = mybir.dt.float32r
BF16 = mybir.dt.bfloat16
I32 = mybir.dt.int32
U32 = mybir.dt.uint32

P = 128
NB = 16
PAIRS = NB // 2
D = 64
HALF = 64
T = P + HALF
NT = 3
PT = NT * P
IMG = 96
NH = 16
NQK = NH + 1
WINDOW = 128
EXPERTS = 32
HID = 16
TOPK = T // 2 - 1
LN_EPS = 1e-5
RMS_EPS = 1.1920929e-07
NEG = -1e30
RSQRT_SEED = 0x5F3759DF

MASK_COLS = dict(mask01=128, mask2=192, b01=128, b21=64, b22=64, a01=128, a21=128, a22=128)
SHAPE_COLS = dict(ident=128, rope=192, iota=32, before=384, resize=32)
WEIGHT_COLS = dict(wo01=512, wo2=512, w1=256, w2=128, wr=128, br=1, b1=2, b2=64, qn=64, kn=64,
                   rout=32, e1=512, e2=256, e2b=64, tok=64)


def offsets(cols):
    at, out = 0, {}
    for name, width in cols.items():
        out[name] = (at, at + width)
        at += width
    return out, at


MASK_AT, MASK_N = offsets(MASK_COLS)
SHAPE_AT, SHAPE_N = offsets(SHAPE_COLS)
WEIGHT_AT, WEIGHT_N = offsets(WEIGHT_COLS)

A_VEC = ["x", "sums1", "stats1", "xn1", "recip", "ctx", "sums2", "stats2", "xn2", "wcol", "equal", "rank", "wsel",
         "y", "yw", "h"]
A_POOL = ["var1", "rstd1", "var2", "rstd2", "hx"]
A_PE = ["xT1", "s01", "s2", "ctx", "xT2", "route", "h1a", "h1b", "y"]
A_ACT = ["xT1", "p01", "p2", "xT2", "route", "h1a", "h1b"]
B_VEC = (["sums", "stats", "xn", "hi", "xs", "ssq0", "ssq1", "ssq2", "ms", "shift", "seed"]
         + [f"{s}{n}" for n in range(3) for s in ("ny", "nx", "n")]
         + ["rope0", "rope1", "rope2", "khi", "klo"])
B_POOL = ["var", "rstd"] + [f"{s}{t}" for s, t in
          [("cs", 0), ("cs", 1), ("rot", 0), ("kw", 0), ("lo", 0), ("cs", 2), ("rot", 1), ("kw", 1), ("lo", 1),
           ("rot", 2), ("kw", 2), ("lo", 2)]]
B_ACT = ["sq0", "sq1", "sq2", "hi0", "hi1", "hi2", "mT"]
RING_Q = ["xT", "q00", "q01", "q10", "q11", "q20", "q21", "kv"] \
    + [f"tq{t}{i}" for t in (0, 1) for i in range(4)] + ["kTh", "kTl"] + [f"tq2{i}" for i in range(4)]
D_VEC = ["h", "sums", "stats", "xn", "logits", "top", "index", "indexf", "onehot", "hm0", "hm1", "hm2", "out"]
D_POOL = ["var", "rstd"]
D_PE = ["y0", "y1", "y2", "xT", "logits", "h0", "h1", "h2", "t0", "t1", "t2", "oneT", "out"]
D_ACT = ["xT", "t0", "t1", "t2", "oneT"]


class Pair:

    def __init__(self, base, n):
        self.par = n % 2
        self.half = base + n // 2
        self.n = base * 2 + n


def after(names, pair, name):
    return pair.n * len(names) + names.index(name) + 1


def wait_apart(eng, semaphore, count):
    if isinstance(count, int):
        eng.wait_ge(semaphore, count)
        return
    count = eng.to_reg(count)
    eng.wait_ge(semaphore, 1)
    eng.wait_ge(semaphore, count)


def part(start, size):
    return slice(start, start + size) if isinstance(start, int) else bass.ds(start, size)


def spread(items, start, end):
    return [(start + (end - start) * (k + 0.5) / len(items), item) for k, item in enumerate(items)]


C_ORDER = ["E0", "E1", "V0", "E2", "V1", "E3", "V2", "E4", "V3", "X0", "E5", "X1", "V4", "E6", "V5", "wo0", "E7", "V6",
           "E8", "V7", "X2", "E9", "X3", "E10", "E11", "wo1", "E12", "V8", "E13", "V9", "X4", "V10", "V11", "X5", "wo2"]
D_ORDER = ["ln", "xT", "logits", "pick", "h0", "h1", "h2", "t0", "t1", "t2", "oneT", "out"]
B_ORDER = ["ln", "xs", "xT", "q00", "q01", "q10", "q11", "q20", "q21", "kv", "sq0", "sq1", "sq2", "rms", "cs0", "cs1",
           "rope0", "rope1", "rot0", "cs2"] + [f"tq0{i}" for i in range(4)] + ["rot1", "rope2"] \
    + [f"tq1{i}" for i in range(4)] + ["rot2", "kk", "kTh", "kTl"] \
    + [f"S{n}" for n in range(8)] + [f"tq2{i}" for i in range(4)] + [f"S{n}" for n in range(8, 16)] + ["mT"]
A_ORDER = ["ln1", "xn1", "xT1", "s01", "s2", "ctx", "ln2", "xn2", "xT2", "route", "rank1", "h1a", "rank2", "h1b",
           "rank3", "y", "h"]


def step_order(with_a, with_b):
    todo = spread([("C", x) for x in C_ORDER], 0.0, 0.62) + spread([("D", x) for x in D_ORDER], 0.64, 1.0)
    if with_b:
        todo += spread([("B", x) for x in B_ORDER], 0.0, 0.98)
    if with_a:
        todo += spread([("A", x) for x in A_ORDER], 0.05, 0.99)
    return [item for _, item in sorted(todo, key=lambda z: z[0])]


def run_program(eng, chunks):
    def run(stage, name, pair):
        f = chunks.get((stage, name))
        if f is not None:
            f(pair)

    def step(base, n, with_a, with_b):
        for stage, name in step_order(with_a, with_b):
            run(stage, name, Pair(base, n + {"A": 2, "B": 1, "C": 0, "D": 0}[stage]))

    for name in A_ORDER:
        run("A", name, Pair(0, 0))
    warm = spread([("B", x, 0) for x in B_ORDER], 0.0, 1.0) + spread([("A", x, 1) for x in A_ORDER], 0.0, 1.0)
    for _, (stage, name, n) in sorted(warm, key=lambda z: z[0]):
        run(stage, name, Pair(0, n))
    with eng.Fori(0, PAIRS // 2 - 1) as i:
        step(i, 0, True, True)
        step(i, 1, True, True)
    step(0, PAIRS - 2, False, True)
    step(0, PAIRS - 1, False, False)


def early_fusion(nc, shapes, masks, weights, wqkv, images, txt, out):
    with ExitStack() as ctx:
        def sb(name, shape, dt=F32):
            return ctx.enter_context(nc.sbuf_tensor(name, shape, dt))

        def sem(name):
            return ctx.enter_context(nc.semaphore(name))

        bank = [ctx.enter_context(nc.psum_tensor(f"bank{n}", [P, 512], F32)) for n in range(8)]
        BANK_D, BANK_Q, BANK_S, BANK_A, BANK_E, BANK_O = 0, (1, 2), 3, 4, (5, 6), 7

        cst = sb("cst", [P, SHAPE_N])
        wts = sb("wts", [P, WEIGHT_N])

        def cs(name):
            if name in MASK_AT:
                return msk[:, MASK_AT[name][0]:MASK_AT[name][1]]
            return cst[:, SHAPE_AT[name][0]:SHAPE_AT[name][1]]

        def wt(name):
            return wts[:, WEIGHT_AT[name][0]:WEIGHT_AT[name][1]]

        ident = cs("ident")
        ident_r = sb("ident_r", [P, P], F32R)
        ident_b = sb("ident_b", [P, P], BF16)
        mask01 = sb("mask01", [P, P], BF16)
        mask2 = sb("mask2", [P, T], BF16)
        wq_hi = sb("wq_hi", [P, 1152], F32R)
        wq_lo = sb("wq_lo", [P, 1152], F32R)
        sh_l01 = sb("sh_l01", [P, P], F32R)
        sh_l21 = sb("sh_l21", [P, P], F32R)
        sh_l22 = sb("sh_l22", [P, P], F32R)
        sh_r01 = sb("sh_r01", [P, 2, NH, P], F32R)
        sh_r21 = sb("sh_r21", [P, 2, NH, HALF], F32R)
        sh_r22 = sb("sh_r22", [P, NH, HALF], F32R)
        wqk = sb("wqk", [P, D])
        minus_half = sb("minus_half", [P, NT])
        ln_eps = sb("ln_eps", [P, NT])
        h0 = sb("h0", [P, PAIRS, NT, D])
        hA = sb("hA", [P, NT, D])
        sumsA = sb("sumsA", [P, NT, 6])
        mvA = sb("mvA", [P, NT, 2])
        rsA = sb("rsA", [P, NT])
        xa = sb("xa", [P, NT, D + 1])
        xpad = sb("xpad", [P, 2, D + 1])
        xaT = sb("xaT", [D, PT])
        h1T = sb("h1T", [P, 2, PT])
        pA01 = h1T[:, 0, :].rearrange("s (b t) -> s b t", b=2)
        pA2 = h1T[:, 1, 0:T]
        recA = sb("recA", [P, NT])
        xf = sb("xf", [P, NT, D])
        xfT = xaT
        hx = sb("hx", [P, NT, D])
        rt = sb("rt", [P, 2, T])
        wcol = sb("wcol", [P, NT])
        eq = sb("eq", [P, NT, T])
        junk = [eq[:, t, 0:P] for t in range(NT)]
        rank = sb("rank", [P, NT])
        wsel = sb("wsel", [P, NT])
        yA = xa[:, :, 0:D]
        hB = [sb(f"hB{u}", [P, NT, D]) for u in range(2)]
        sumsB = sb("sumsB", [P, NT, 6])
        mvB = sb("mvB", [P, NT, 2])
        rsB = sb("rsB", [P, NT])
        xsT = sb("xsT", [P, PT], F32R)
        q_sb = sb("q_sb", [P, NT, NQK, D])
        ssq = sb("ssq", [P, NT, NQK])
        nx = sb("nx", [P, NT * NQK])
        ny = sb("ny", [P, NT * NQK])
        nt_ = sb("nt_", [P, NT * NQK])
        nu = sb("nu", [P, NT * NQK])
        csr = sb("csr", [P, 2, NQK, D])
        ta = q_sb
        tb = sb("tb", [P, 2, NQK, D])
        sq = tb
        kk = sb("kk", [P, NT, D])
        xb = tb[:, 0, 0:NT, :]
        ks = sb("ks", [P, 2, NT, 2, D], F32R)
        xs = ks[:, 0, :, :, :].rearrange("q t c d -> q t (c d)")
        qs = sb("qs", [P, NH, 2 * D], F32R)
        qT = [sb(f"qT{u}", [P, NT, NH, P], F32R) for u in range(2)]
        qT2 = [q[:, 2, :, :].rearrange("k h t -> k (h t)").rearrange("k (b h t) -> k b h t", b=2, h=NH) for q in qT]
        kh = [sb(f"kh{u}", [P, 2, T], F32R) for u in range(2)]
        kl = [sb(f"kl{u}", [P, 2, P], F32R) for u in range(2)]
        kp = [sb(f"kp{u}", [P, 2, 2, P], F32R) for u in range(2)]
        vx = [sb(f"vx{u}", [P, 2, D + 1]) for u in range(2)]
        vp = [sb(f"vp{u}", [P, 2, D + 1]) for u in range(2)]
        negm = sb("negm", [P, 48])
        mT = sb("mT", [48, P], F32R)
        p01 = sb("p01", [P, 3, 4, P])
        p21 = sb("p21", [P, 2, NH, HALF])
        p22 = sb("p22", [P, NH, HALF])
        rec = sb("rec", [P, 4])
        on = sb("on", [P, NH, D])
        oT = sb("oT", [P, NH // 2, P])
        early = q_sb[:, :, :, :].rearrange("q t h d -> q (t h d)")
        img = early[0:IMG, 0:NB * IMG].rearrange("r (b c) -> r b c", b=NB)
        z_sb = early[0:IMG, NB * IMG:NB * IMG + NB * 32]
        w_raw = early[:, 2048:2048 + 1152]
        early21 = p21[:, :, :, :].rearrange("q b h t -> q (b h t)")
        feat_ib = early21[0:8, 0:NB * D].rearrange("m (i b j) -> m i b j", b=NB, i=8)
        feat = tb[0:8, 0, 0:NH, :].rearrange("m b (i j) -> m b i j", i=8)
        msk = early21[:, NB * D:NB * D + MASK_N]
        f_sb = p22[0:32, :, :].rearrange("m h t -> m (h t)")[:, 0:NB * 32].rearrange("m (o b j) -> m o b j", b=NB, j=8)
        hC = sb("hC", [P, NT, D])
        sumsD = sb("sumsD", [P, NT, 6])
        mvD = sb("mvD", [P, NT, 2])
        rsD = sb("rsD", [P, NT])
        xd = on[:, 0:NT, :]
        xdT = sb("xdT", [D + 1, PT])
        small = p22[:, :, :].rearrange("q h t -> q (h t)")
        lg = small[:, 0:96].rearrange("q (t e) -> q t e", t=NT)
        top = sb("top", [P, NT, 8])
        ix = sb("ix", [P, NT, 8], U32)
        ixf = sb("ixf", [P, NT])
        one_hot = small[:, 128:224].rearrange("q (t e) -> q t e", t=NT)
        hm = p01[:, :, :, :].rearrange("q t c k -> q t (c k)")
        hmT = early21[:, 0:NT * 4 * P].rearrange("k (t c q) -> k t c q", t=NT, c=4)
        ohT = small[0:EXPERTS, 256:256 + PT]
        o_sb = [sb(f"o_sb{u}", [P, NT, D]) for u in range(2)]

        ld_w, ld_img, ld_txt = sem("ld_w"), sem("ld_img"), sem("ld_txt")
        set_vec, set_pool, set_act = sem("set_vec"), sem("set_pool"), sem("set_act")
        tok_pe, tok_act, tok_vec, feat_dma = sem("tok_pe"), sem("tok_act"), sem("tok_vec"), sem("feat_dma")
        a_vec, a_pool, a_pe, a_act = sem("a_vec"), sem("a_pool"), sem("a_pe"), sem("a_act")
        b_vec, b_pool, b_act = sem("b_vec"), sem("b_pool"), sem("b_act")
        ring_pe, ring_act = sem("ring_pe"), sem("ring_act")
        s_pe, s_vec, mt_pe = sem("s_pe"), sem("s_vec"), sem("mt_pe")
        m_row = [sem("m_row0"), sem("m_row1")]
        e_pe, e_act = sem("e_pe"), sem("e_act")
        o_pe, o_rec, o_vec = sem("o_pe"), sem("o_rec"), sem("o_vec")
        x_pe, x_act = sem("x_pe"), sem("x_act")
        d_vec, d_pool, d_pe, d_act = sem("d_vec"), sem("d_pool"), sem("d_pe"), sem("d_act")
        stored = [sem("stored0"), sem("stored1")]

        SET_VEC, SET_POOL, SET_ACT = 3, 1, 1
        M_DMAS, OUT_DMAS = 6, 3

        block = ctx.enter_context(nc.Block())

        @block.sync
        def _(sp):
            sp.dma_start(cst[:, :], shapes).then_inc(ld_w, 16)
            sp.dma_start(img, images).then_inc(ld_img, 16)
            sp.dma_start(msk, masks).then_inc(ld_w, 16)
            sp.dma_start(w_raw, wqkv).then_inc(ld_w, 16)
            sp.dma_start(wts[:, :], weights).then_inc(ld_w, 16)
            tv = txt.rearrange("(p k) t d -> k t p d", k=2)
            for k in range(2):
                sp.dma_start(h0[64:128, :, k, :], tv[k, 0:64]).then_inc(ld_txt, 16)
                sp.dma_start(h0[64 * k:64 * k + 64, :, 2, :], tv[k, 64:128]).then_inc(ld_txt, 16)
            sp.wait_ge(tok_act, 2)
            sp.wait_ge(set_vec, SET_VEC)
            for m, (o_r, o_c) in enumerate([(0, 0), (1, 0), (0, 1), (1, 1), (3, 2), (2, 3), (3, 3)]):
                sp.dma_start(feat_ib[m:m + 1, :, :, :].rearrange("m i b j -> m i (b j)"),
                             f_sb[8 * o_r:8 * o_r + 8, o_c, :, :].rearrange("i b j -> i (b j)")).then_inc(feat_dma, 16)

            def m_rows(pair):
                u = pair.par
                sp.wait_ge(b_act, after(B_ACT, pair, "mT"))
                r01, r21, r22 = (r.bitcast(F32) for r in (sh_r01[:, :, :, :], sh_r21[:, :, :, :], sh_r22[:, :, :]))
                rows_of = mT[:, :].bitcast(F32)
                for b in range(2):
                    sp.dma_start(r01[0:1, b, :, :], rows_of[16 * b:16 * b + 16, :]).then_inc(m_row[u], 16)
                    rows = rows_of[32 + 8 * b:40 + 8 * b, :]
                    sp.dma_start(r21[127:128, b, :, :].rearrange("o h t -> o (h t)"), rows).then_inc(m_row[u], 16)
                    sp.dma_start(r22[64 * b:64 * b + 1, :, :].rearrange("o h t -> o (h t)"), rows).then_inc(m_row[u], 16)

            def store(pair):
                sp.wait_ge(d_vec, after(D_VEC, pair, "out"))
                o = o_sb[pair.par]
                two = out[part(pair.n * 2, 2), :, :]
                sp.dma_start(two[:, 0:P, :].rearrange("b t d -> t b d"), o[:, 0:2, :]).then_inc(stored[pair.par], 16)
                for k in range(2):
                    sp.dma_start(out[part(pair.n * 2 + k, 1), P:T, :].rearrange("b t d -> t b d"),
                                 o[64 * k:64 * k + 64, 2:3, :]).then_inc(stored[pair.par], 16)

            run_program(sp, {("B", "mT"): m_rows, ("D", "out"): store})
            for u in range(2):
                sp.wait_ge(stored[u], 16 * OUT_DMAS * PAIRS // 2)

        def tiles(ap):
            return [ap[:, t, :] for t in range(NT)]

        @block.vector
        def _(ve):
            n_set = [0]

            def then_wait(ins):
                n_set[0] += 1
                ins.then_inc(set_vec, 1)
                ve.wait_ge(set_vec, n_set[0])

            then_wait(ve.memset(feat_ib, 1.0))
            ve.memset(xdT[D:D + 1, :], 1.0)
            ve.wait_ge(set_pool, 1)
            for b in range(2):
                h = slice(64 * b, 64 * b + 64)
                ve.memset(xpad[h, b, D:D + 1], 1.0)
                for u in range(2):
                    ve.memset(vp[u][h, b, D:D + 1], 1.0)
            ve.wait_ge(ld_w, 64)
            ve.tensor_copy(ident_r[:, :], ident)
            ve.tensor_copy(ident_b[:, :], ident)
            ve.tensor_copy(mask01[:, :], cs("mask01"))
            ve.tensor_copy(mask2[:, :], cs("mask2"))
            ve.tensor_copy(sh_l01[:, :], cs("a01"))
            ve.tensor_copy(sh_l21[:, :], cs("a21"))
            ve.tensor_copy(sh_l22[:, :], cs("a22"))
            ve.tensor_scalar(wqk[:, :], wt("qn"), float(D) ** -0.5, None, ALU.mult)
            then_wait(ve.tensor_copy(wq_hi[:, :], w_raw))
            ve.tensor_tensor(wqk[:, :], wqk[:, :], wt("kn"), ALU.mult)
            then_wait(ve.tensor_tensor(wq_lo[:, :], w_raw, wq_hi[:, :].bitcast(F32), ALU.subtract))

            for g in range(2):
                ve.wait_ge(tok_pe, 3 + g)
                ve.tensor_copy(h0[0:64, 4 * g:4 * g + 4, 0:2, :],
                               bank[BANK_E[g]][0:64, :].rearrange("t (p k d) -> t p k d", k=2, d=D)).then_inc(tok_vec, 1)
            ve.wait_ge(ld_txt, 64)
            ve.wait_ge(tok_vec, 2)

            def sums(src, buf, done):
                for t in range(NT):
                    ins = ve.bn_stats(buf[:, t, :], src[:, t, :])
                ins.then_inc(done, 1)

            def stats(buf, mv, done):
                for t in range(NT):
                    ins = ve.bn_aggr(mv[:, t, :], buf[:, t, :])
                ins.then_inc(done, 1)

            def normalise(dst, src, mv, rs, done):
                for t in range(NT):
                    ins = ve.tensor_scalar(dst[:, t, 0:D], src[:, t, :], mv[:, t, 0:1], rs[:, t:t + 1],
                                           ALU.subtract, ALU.mult)
                if done is not None:
                    ins.then_inc(done, 1)

            bA = bank[BANK_A]

            def a_ln1(p):
                ve.tensor_copy(hA[:, :, :], h0[:, part(p.n, 1), :, :].rearrange("q o t d -> q (o t) d")).then_inc(a_vec, 1)
                ve.wait_ge(a_vec, after(A_VEC, p, "x"))
                sums(hA, sumsA, a_vec)
                wait_apart(ve, a_vec, after(A_VEC, p, "sums1"))
                stats(sumsA, mvA, a_vec)

            def a_xn1(p):
                ve.wait_ge(a_pool, after(A_POOL, p, "rstd1"))
                normalise(xa, hA, mvA, rsA, None)
                for b in range(2):
                    h = slice(64 * b, 64 * b + 64)
                    ins = ve.tensor_scalar(xpad[h, b, 0:D], hA[h, 2, :], mvA[h, 2, 0:1], rsA[h, 2:3],
                                           ALU.subtract, ALU.mult)
                ins.then_inc(a_vec, 1)

            def a_ctx(p):
                o = bA[:, 0:NT * (D + 1)].rearrange("q (t d) -> q t d", t=NT)
                ve.wait_ge(a_pe, after(A_PE, p, "ctx"))
                ve.reciprocal(recA[:, :], o[:, :, D]).then_inc(a_vec, 1)
                ve.wait_ge(a_vec, after(A_VEC, p, "recip"))
                for t in range(NT):
                    ins = ve.scalar_tensor_tensor(hA[:, t, :], o[:, t, 0:D], recA[:, t:t + 1], hA[:, t, :],
                                                  ALU.mult, ALU.add)
                ins.then_inc(a_vec, 1)

            def a_ln2(p):
                ve.wait_ge(a_vec, after(A_VEC, p, "ctx"))
                sums(hA, sumsA, a_vec)
                wait_apart(ve, a_vec, after(A_VEC, p, "sums2"))
                stats(sumsA, mvA, a_vec)

            def a_xn2(p):
                ve.wait_ge(a_pool, after(A_POOL, p, "rstd2"))
                normalise(xf, hA, mvA, rsA, a_vec)

            halves = [(slice(0, P), 0, 0, 0), (slice(0, P), 1, 1, 0), (slice(0, 64), 0, 2, 1), (slice(64, P), 1, 2, 1)]
            before = cs("before").rearrange("q (k s) -> q k s", k=2)

            def a_rank1(p):
                ve.wait_ge(a_act, after(A_ACT, p, "route"))
                for t in range(2):
                    ve.tensor_tensor_reduce(junk[t], rt[:, t, 0:P], ident, 1.0, 0.0, ALU.mult, ALU.add,
                                            wcol[:, t:t + 1])
                ve.tensor_tensor_reduce(junk[2].rearrange("q (k s) -> q k s", k=2), rt[:, :, P:T],
                                        ident.rearrange("q (k s) -> q k s", k=2), 1.0, 0.0, ALU.mult, ALU.add,
                                        wcol[:, 2:3]).then_inc(a_vec, 1)

            def a_rank2(p):
                ve.wait_ge(a_vec, after(A_VEC, p, "wcol"))
                for q, b, t, k in halves:
                    ins = ve.scalar_tensor_tensor(eq[q, t, :], rt[q, b, :], wcol[q, t:t + 1], before[q, k, :],
                                                  ALU.is_equal, ALU.mult)
                ins.then_inc(a_vec, 1)

            def a_rank3(p):
                ve.wait_ge(a_vec, after(A_VEC, p, "equal"))
                for q, b, t, k in halves:
                    ins = ve.scalar_tensor_tensor(eq[q, t, :], rt[q, b, :], wcol[q, t:t + 1], eq[q, t, :],
                                                  ALU.is_gt, ALU.add, accum_out=rank[q, t:t + 1])
                ins.then_inc(a_vec, 1)
                ve.wait_ge(a_vec, after(A_VEC, p, "rank"))
                ve.scalar_tensor_tensor(wsel[:, :], rank[:, :], TOPK - 0.5, wcol[:, :], ALU.is_lt, ALU.mult).then_inc(a_vec, 1)

            def a_y(p):
                ve.wait_ge(a_pe, after(A_PE, p, "y"))
                ve.tensor_tensor(yA, bA[:, 0:NT * D].rearrange("q (t d) -> q t d", t=NT),
                                 wt("b2").unsqueeze(1).broadcast_to([P, NT, D]), ALU.add).then_inc(a_vec, 1)
                ve.wait_ge(a_vec, after(A_VEC, p, "y"))
                ve.tensor_tensor(yA, yA, wsel[:, :].unsqueeze(2).broadcast_to([P, NT, D]),
                                 ALU.mult).then_inc(a_vec, 1)

            def a_h(p):
                ve.wait_ge(a_vec, after(A_VEC, p, "yw"))
                ve.wait_ge(a_pool, after(A_POOL, p, "hx"))
                ve.tensor_tensor(hB[p.par][:, :, :], hx[:, :, :], yA, ALU.add).then_inc(a_vec, 1)

            def b_ln(p):
                ve.wait_ge(a_vec, after(A_VEC, p, "h"))
                sums(hB[p.par], sumsB, b_vec)
                wait_apart(ve, b_vec, after(B_VEC, p, "sums"))
                stats(sumsB, mvB, b_vec)

            def b_xs(p):
                ve.wait_ge(b_pool, after(B_POOL, p, "rstd"))
                normalise(xb, hB[p.par], mvB, rsB, b_vec)
                ve.wait_ge(b_vec, after(B_VEC, p, "xn"))
                ve.tensor_copy(xs[:, :, 0:D], xb[:, :, :]).then_inc(b_vec, 1)
                ve.wait_ge(b_vec, after(B_VEC, p, "hi"))
                ve.tensor_tensor(xs[:, :, D:2 * D], xb[:, :, :], xs[:, :, 0:D].bitcast(F32), ALU.subtract).then_inc(b_vec, 1)

            def b_sq(t):
                def f(p):
                    ve.wait_ge(b_act, after(B_ACT, p, f"sq{t}"))
                    ve.tensor_reduce(ssq[:, t, :], sq[:, t % 2, :, :], AX_X, ALU.add).then_inc(b_vec, 1)
                return f

            def b_rms(p):
                ve.wait_ge(b_vec, after(B_VEC, p, "ssq2"))
                ve.tensor_scalar(nx[:, :], ssq[:, :, :].rearrange("q t h -> q (t h)"), 1.0 / D, RMS_EPS,
                                 ALU.mult, ALU.add).then_inc(b_vec, 1)
                ve.wait_ge(b_vec, after(B_VEC, p, "ms"))
                ve.tensor_scalar(nu[:, :].bitcast(I32), nx[:, :].bitcast(I32), 1, None,
                                 ALU.logical_shift_right).then_inc(b_vec, 1)
                ve.wait_ge(b_vec, after(B_VEC, p, "shift"))
                ve.tensor_scalar(ny[:, :].bitcast(I32), nu[:, :].bitcast(I32), -1.0, float(RSQRT_SEED),
                                 ALU.mult, ALU.add).then_inc(b_vec, 1)
                ve.wait_ge(b_vec, after(B_VEC, p, "seed"))
                for n in range(3):
                    ve.scalar_tensor_tensor(nt_[:, :], ny[:, :], -0.5, ny[:, :], ALU.mult, ALU.mult).then_inc(b_vec, 1)
                    ve.wait_ge(b_vec, after(B_VEC, p, f"ny{n}"))
                    ve.tensor_tensor(nu[:, :], nt_[:, :], nx[:, :], ALU.mult).then_inc(b_vec, 1)
                    ve.wait_ge(b_vec, after(B_VEC, p, f"nx{n}"))
                    ve.scalar_tensor_tensor(ny[:, :], nu[:, :], 1.5, ny[:, :], ALU.add, ALU.mult).then_inc(b_vec, 1)
                    if n < 2:
                        ve.wait_ge(b_vec, after(B_VEC, p, f"n{n}"))

            def b_rope(t):
                def f(p):
                    ve.wait_ge(b_pool, after(B_POOL, p, f"cs{t}"))
                    q = q_sb[:, t, :, :].rearrange("q h (i c) -> q h i c", c=2)
                    if t == 2:
                        ve.wait_ge(b_pool, after(B_POOL, p, "rot0"))
                    for dst, k in ((tb[:, t % 2, :, :], 1), (ta[:, t, :, :], 0)):
                        ins = ve.tensor_tensor(dst.rearrange("q h (i c) -> q h i c", c=2), q,
                                               csr[:, t % 2, :, 32 * k:32 * k + 32].unsqueeze(3)
                                               .broadcast_to([P, NQK, 32, 2]), ALU.mult)
                    ins.then_inc(b_vec, 1)
                return f

            def b_kk(p):
                ve.wait_ge(b_pool, after(B_POOL, p, "kw2"))
                k2 = kk[:, :, :].unsqueeze(2).broadcast_to([P, NT, 2, D])
                ve.tensor_copy(ks[:, 0, :, :, :], k2).then_inc(b_vec, 1)
                ve.wait_ge(b_vec, after(B_VEC, p, "khi"))
                ve.tensor_tensor(ks[:, 1, :, :, :], k2, ks[:, 0, :, :, :].bitcast(F32), ALU.subtract).then_inc(b_vec, 1)

            def b_s(n):
                def f(p):
                    ve.wait_ge(s_pe, p.n * 16 + n + 1)
                    if n < 8:
                        src = bank[BANK_S][:, :].rearrange("q (h s) -> q h s", h=4)
                        dst = negm[:, 4 * n:4 * n + 4]
                    else:
                        src = bank[BANK_S][:, 0:2 * T].rearrange("q (h s) -> q h s", h=2)
                        dst = negm[:, 32 + 2 * (n - 8):34 + 2 * (n - 8)]
                    ve.tensor_reduce(dst, src, AX_X, ALU.max, negate=True).then_inc(s_vec, 1)
                return f

            def c_v(v):
                def f(p):
                    o = bank[BANK_O][:, 0:4 * (D + 1)].rearrange("q (h d) -> q h d", h=4)
                    ve.wait_ge(o_pe, p.n * 12 + v + 1)
                    ve.reciprocal(rec[:, :], o[:, :, D]).then_inc(o_rec, 1)
                    ve.wait_ge(o_rec, p.n * 12 + v + 1)
                    ve.tensor_tensor(on[:, 4 * (v % 4):4 * (v % 4) + 4, :], o[:, :, 0:D], rec[:, :].unsqueeze(2).broadcast_to([P, 4, D]),
                                     ALU.mult).then_inc(o_vec, 1)
                return f

            def tile3(n, w):
                return bank[BANK_D][:, 0:n * w].rearrange("q (t d) -> q t d", t=n)

            def d_wo(p):
                ve.wait_ge(d_pe, after(D_PE, p, "y2"))
                ve.tensor_tensor(hC[:, :, :], tile3(NT, D), hB[p.par][:, :, :], ALU.add).then_inc(d_vec, 1)

            def d_ln(p):
                ve.wait_ge(d_vec, after(D_VEC, p, "h"))
                sums(hC, sumsD, d_vec)
                wait_apart(ve, d_vec, after(D_VEC, p, "sums"))
                stats(sumsD, mvD, d_vec)

            def d_xt(p):
                ve.wait_ge(d_pool, after(D_POOL, p, "rstd"))
                normalise(xd, hC, mvD, rsD, d_vec)

            def d_logits(p):
                ve.wait_ge(d_pe, after(D_PE, p, "logits"))
                ve.tensor_copy(lg, tile3(NT, EXPERTS)).then_inc(d_vec, 1)

            def d_pick(p):
                wait_apart(ve, d_vec, after(D_VEC, p, "logits"))
                for t in range(NT):
                    ins = ve.max(top[:, t, :], lg[:, t, :])
                ins.then_inc(d_vec, 1)
                wait_apart(ve, d_vec, after(D_VEC, p, "top"))
                for t in range(NT):
                    ins = ve.max_index(ix[:, t, :], top[:, t, :], lg[:, t, :])
                ins.then_inc(d_vec, 1)
                ve.wait_ge(d_vec, after(D_VEC, p, "index"))
                ve.tensor_copy(ixf[:, :], ix[:, :, 0]).then_inc(d_vec, 1)
                ve.wait_ge(d_vec, after(D_VEC, p, "indexf"))
                ve.tensor_tensor(one_hot, cs("iota").unsqueeze(1).broadcast_to([P, NT, EXPERTS]),
                                 ixf[:, :].unsqueeze(2).broadcast_to([P, NT, EXPERTS]), ALU.is_equal).then_inc(d_vec, 1)

            def d_hm(t):
                def f(p):
                    if t == 0:
                        ve.wait_ge(d_vec, after(D_VEC, p, "onehot"))
                    ve.wait_ge(d_pe, after(D_PE, p, f"h{t}"))
                    ve.scalar_tensor_tensor(hm[:, t, :].rearrange("q (e j) -> q e j", e=EXPERTS),
                                            bank[BANK_D][:, :].rearrange("q (e j) -> q e j", e=EXPERTS), 0.0,
                                            one_hot[:, t, :].unsqueeze(2).broadcast_to([P, EXPERTS, HID]),
                                            ALU.max, ALU.mult).then_inc(d_vec, 1)
                return f

            def d_out(p):
                ve.wait_ge(d_pe, after(D_PE, p, "out"))
                ve.wait_ge(stored[p.par], p.half * (16 * OUT_DMAS))
                ve.scalar_tensor_tensor(o_sb[p.par][:, :, :], tile3(NT, D), 0.0, hC[:, :, :], ALU.max,
                                        ALU.add).then_inc(d_vec, 1)

            run_program(ve, {
                ("A", "ln1"): a_ln1, ("A", "xn1"): a_xn1, ("A", "ctx"): a_ctx, ("A", "ln2"): a_ln2, ("A", "xn2"): a_xn2,
                ("A", "rank1"): a_rank1, ("A", "rank2"): a_rank2, ("A", "rank3"): a_rank3, ("A", "y"): a_y, ("A", "h"): a_h,
                ("B", "ln"): b_ln, ("B", "xs"): b_xs, ("B", "rms"): b_rms, **{("B", f"sq{t}"): b_sq(t) for t in range(NT)}, ("B", "kk"): b_kk,
                **{("B", f"rope{t}"): b_rope(t) for t in range(NT)},
                **{("B", f"S{n}"): b_s(n) for n in range(16)},
                **{("C", f"V{v}"): c_v(v) for v in range(12)},
                ("C", "wo2"): d_wo, ("D", "ln"): d_ln, ("D", "xT"): d_xt, ("D", "logits"): d_logits, ("D", "pick"): d_pick,
                **{("D", f"h{t}"): d_hm(t) for t in range(NT)}, ("D", "out"): d_out})

        @block.gpsimd
        def _(gp):
            gp.memset(xa[:, :, :], 1.0)
            gp.memset(xpad[:, :, :], 0.0)
            for u in range(2):
                gp.memset(vx[u][:, :, :], 1.0)
                gp.memset(vp[u][:, :, :], 0.0)
                gp.memset(kp[u][:, :, :, :].bitcast(F32), 0.0)
            gp.memset(ln_eps[:, :], LN_EPS)
            gp.memset(minus_half[:, :], -0.5).then_inc(set_pool, 1)
            gp.wait_ge(ld_w, 64)
            for b in range(2):
                gp.tensor_copy(sh_r21[:, b, :, :], cs("b21").unsqueeze(1).broadcast_to([P, NH, HALF]))
            ins = gp.tensor_copy(sh_r22[:, :, :], cs("b22").unsqueeze(1).broadcast_to([P, NH, HALF]))
            ins.then_inc(set_pool, 1)

            def rstd(mv, rs, sem_pool, names, p, var):
                gp.tensor_tensor(rs[:, :], mv[:, :, 1], ln_eps[:, :], ALU.add).then_inc(sem_pool, 1)
                gp.wait_ge(sem_pool, after(names, p, var))
                gp.tensor_tensor(rs[:, :], rs[:, :], minus_half[:, :], ALU.pow).then_inc(sem_pool, 1)

            def a_ln1(p):
                gp.wait_ge(a_vec, after(A_VEC, p, "stats1"))
                rstd(mvA, rsA, a_pool, A_POOL, p, "var1")

            def a_ln2(p):
                gp.wait_ge(a_vec, after(A_VEC, p, "stats2"))
                rstd(mvA, rsA, a_pool, A_POOL, p, "var2")

            def a_hx(p):
                gp.wait_ge(a_vec, after(A_VEC, p, "xn2"))
                gp.tensor_tensor(hx[:, :, :], hA[:, :, :], xf[:, :, :], ALU.add).then_inc(a_pool, 1)

            def b_ln(p):
                gp.wait_ge(b_vec, after(B_VEC, p, "stats"))
                rstd(mvB, rsB, b_pool, B_POOL, p, "var")

            rope = cs("rope").rearrange("q (t c) -> q t c", t=NT)

            def b_cs(t):
                def f(p):
                    if t == 0:
                        gp.wait_ge(b_vec, after(B_VEC, p, "n2"))
                    rq = ny[:, NQK * t:NQK * t + NQK]
                    gp.tensor_tensor(csr[:, t % 2, :, :], rope[:, t, :].unsqueeze(1).broadcast_to([P, NQK, D]),
                                     rq.unsqueeze(2).broadcast_to([P, NQK, D]), ALU.mult).then_inc(b_pool, 1)
                return f

            def b_rot(t):
                def f(p):
                    gp.wait_ge(b_vec, after(B_VEC, p, f"rope{t}"))
                    a = ta[:, t, :, :].rearrange("q h (i c) -> q (h i) c", c=2)
                    b = tb[:, t % 2, :, :].rearrange("q h (i c) -> q (h i) c", c=2)
                    gp.tensor_tensor(a[:, :, 0], a[:, :, 0], b[:, :, 1], ALU.subtract)
                    gp.tensor_tensor(a[:, :, 1], a[:, :, 1], b[:, :, 0], ALU.add).then_inc(b_pool, 1)
                    gp.wait_ge(b_pool, after(B_POOL, p, f"rot{t}"))
                    gp.tensor_tensor(kk[:, t, :], ta[:, t, NH, :], wqk[:, :], ALU.mult).then_inc(b_pool, 1)
                    gp.wait_ge(b_act, after(B_ACT, p, f"hi{t}"))
                    gp.tensor_tensor(qs[:, :, D:2 * D], ta[:, t, 0:NH, :], qs[:, :, 0:D].bitcast(F32),
                                     ALU.subtract).then_inc(b_pool, 1)
                return f

            def d_ln(p):
                gp.wait_ge(d_vec, after(D_VEC, p, "stats"))
                rstd(mvD, rsD, d_pool, D_POOL, p, "var")

            gp.wait_ge(set_vec, SET_VEC)
            run_program(gp, {("A", "ln1"): a_ln1, ("A", "ln2"): a_ln2, ("A", "xn2"): a_hx, ("B", "ln"): b_ln,
                             **{("B", f"cs{t}"): b_cs(t) for t in range(NT)},
                             **{("B", f"rot{t}"): b_rot(t) for t in range(NT)}, ("D", "ln"): d_ln})

        @block.scalar
        def _(ac):
            def copy(dst, src):
                return ac.activation(dst, src, ACT.Copy)

            ac.wait_ge(ld_w, 64)
            copy(sh_r01[:, :, :, :].rearrange("j b h t -> j (b h) t"),
                 cs("b01").unsqueeze(1).broadcast_to([P, 2 * NH, P])).then_inc(set_act, 1)
            ac.wait_ge(tok_pe, 1)
            copy(z_sb, bank[BANK_E[0]][0:IMG, :]).then_inc(tok_act, 1)
            ac.wait_ge(tok_pe, 2)
            copy(f_sb, bank[BANK_E[1]][0:32, :].rearrange("m (b o j) -> m o b j", b=NB, j=8)).then_inc(tok_act, 1)
            ac.wait_ge(feat_dma, 16 * 7)
            copy(feat, feat_ib.rearrange("m i b j -> m b i j")).then_inc(tok_act, 1)
            ac.nop().then_inc(ring_act, 2)
            ac.nop().then_inc(e_act, 2)
            ac.wait_ge(set_pool, 2)

            bA, bD, bO = bank[BANK_A], bank[BANK_D], bank[BANK_O]

            def a_do(name, dst, src, func=ACT.Copy, **kw):
                def f(p):
                    ac.wait_ge(a_pe, after(A_PE, p, name[0]))
                    ac.activation(dst, src, func, **kw).then_inc(a_act, 1)
                return f

            def a_h1(c):
                return a_do(["h1a", "h1b"][c:c + 1], h1T[:, c, :], bA[:, 0:PT], ACT.Gelu_apprx_tanh,
                            bias=wt("b1")[:, c:c + 1])

            def unit(p, name):
                ac.wait_ge(ring_pe, after(RING_Q, p, name))
                return bank[BANK_Q[RING_Q.index(name) % 2]]

            def b_xt(p):
                copy(xsT[:, :], unit(p, "xT")[:, 0:PT].bitcast(F32R).bitcast(F32)).then_inc(ring_act, 1)

            def b_q(t, k):
                def f(p):
                    if t == 0 and k == 0 :
                        ac.wait_ge(b_pool, p.n * len(B_POOL))
                    copy(q_sb[:, t, 8 * k:8 * k + 8, :].rearrange("q h d -> q (h d)"),
                         unit(p, f"q{t}{k}")[:, :]).then_inc(ring_act, 1)
                return f

            def b_kv(p):
                b = unit(p, "kv")[:, 0:NT * 2 * D].rearrange("q (t n) -> q t n", t=NT)
                copy(q_sb[:, :, NH, :], b[:, :, 0:D])
                copy(vx[p.par][:, :, 0:D], b[:, 0:2, D:2 * D])
                copy(vp[p.par][0:64, 0, 0:D], b[0:64, 2, D:2 * D])
                copy(vp[p.par][64:128, 1, 0:D], b[64:128, 2, D:2 * D]).then_inc(ring_act, 1)

            def b_sq(t):
                def f(p):
                    if t == 0:
                        ac.wait_ge(ring_act, after(RING_Q, p, "kv") + 2)
                    if t == 2:
                        ac.wait_ge(b_vec, after(B_VEC, p, "ssq0"))
                    ac.activation(sq[:, t % 2, :, :], q_sb[:, t, :, :], ACT.Square).then_inc(b_act, 1)
                return f

            def b_rot(t):
                def f(p):
                    ac.wait_ge(b_pool, after(B_POOL, p, f"rot{t}"))
                    copy(qs[:, :, 0:D], ta[:, t, 0:NH, :]).then_inc(b_act, 1)
                return f

            def b_kth(p):
                b = unit(p, "kTh")
                u = p.par
                halves2 = b[:, 2 * P:3 * P].rearrange("k (b s) -> k b s", b=2)
                copy(kh[u][:, :, 0:P], b[:, 0:2 * P].rearrange("k (b s) -> k b s", b=2))
                copy(kh[u][:, :, P:T], halves2)
                copy(kp[u][:, 0, 0, 0:64], b[:, 2 * P:2 * P + 64])
                copy(kp[u][:, 0, 1, 64:128], b[:, 2 * P + 64:3 * P]).then_inc(ring_act, 1)

            def b_ktl(p):
                b = unit(p, "kTl")
                u = p.par
                copy(kl[u][:, :, :].rearrange("k b s -> k (b s)"), b[:, 0:2 * P])
                copy(kp[u][:, 1, 0, 0:64], b[:, 2 * P:2 * P + 64])
                copy(kp[u][:, 1, 1, 64:128], b[:, 2 * P + 64:3 * P]).then_inc(ring_act, 1)

            def b_tq(t, i):
                def f(p):
                    b = unit(p, f"tq{t}{i}")[:, :]
                    if t < 2:
                        copy(qT[p.par][:, t, 4 * i:4 * i + 4, :].rearrange("k h t -> k (h t)"), b).then_inc(ring_act, 1)
                    else:
                        copy(qT2[p.par][:, :, 4 * i:4 * i + 4, :], b.rearrange("k (h b t) -> k b h t", h=4, b=2)) \
                            .then_inc(ring_act, 1)
                return f

            def b_mt(p):
                ac.wait_ge(mt_pe, p.n + 1)
                copy(mT[:, :], bank[BANK_S][0:48, 0:P]).then_inc(b_act, 1)

            def c_e(n):
                if n < 8:
                    dst = p01[:, n % 3, :, :]
                elif n < 12:
                    dst = p21[:, (n - 8) // 2, 8 * (n % 2):8 * (n % 2) + 8, :]
                else:
                    dst = p22[:, 8 * (n % 2):8 * (n % 2) + 8, :]

                def f(p):
                    if 3 <= n < 8:
                        ac.wait_ge(o_pe, p.n * 12 + n - 2)
                    ac.wait_ge(e_pe, p.n * 14 + n + 1)
                    ac.activation(dst.rearrange("s h t -> s (h t)"), bank[BANK_E[n % 2]][:, :], ACT.Exp).then_inc(e_act, 1)
                return f

            def c_x(n):
                dst = oT[:, 4 * (n % 2):4 * (n % 2) + 4, :]

                def f(p):
                    if n in (2, 4):
                        ac.wait_ge(d_pe, after(D_PE, p, f"y{n // 2 - 1}"))
                    ac.wait_ge(x_pe, p.n * 6 + n + 1)
                    copy(dst.rearrange("k h t -> k (h t)"), bO[:, :]).then_inc(x_act, 1)
                return f

            def d_do(name, dst, src):
                def f(p):
                    ac.wait_ge(d_pe, after(D_PE, p, name))
                    copy(dst, src).then_inc(d_act, 1)
                return f

            run_program(ac, {
                ("A", "xT1"): a_do(["xT1"], xaT[:, :], bA[0:D, 0:PT]),
                ("A", "s01"): a_do(["s01"], pA01[:, :, :].rearrange("s b t -> s (b t)"), bA[:, 0:2 * T], ACT.Exp, scale=D ** -0.5),
                ("A", "s2"): a_do(["s2"], pA2[:, :], bA[:, 0:T], ACT.Exp, scale=D ** -0.5),
                ("A", "xT2"): a_do(["xT2"], xfT[:, :], bA[0:D, 0:PT]),
                ("A", "route"): a_do(["route"], rt[:, :, :].rearrange("q b t -> q (b t)"), bA[:, 0:2 * T], ACT.Identity,
                                     bias=wt("br")),
                ("A", "h1a"): a_h1(0), ("A", "h1b"): a_h1(1),
                ("B", "xT"): b_xt, **{("B", f"q{t}{k}"): b_q(t, k) for t in range(NT) for k in range(2)},
                ("B", "kv"): b_kv, **{("B", f"sq{t}"): b_sq(t) for t in range(NT)}, **{("B", f"rot{t}"): b_rot(t) for t in range(NT)},
                ("B", "kTh"): b_kth, ("B", "kTl"): b_ktl,
                **{("B", f"tq{t}{i}"): b_tq(t, i) for t in range(NT) for i in range(4)}, ("B", "mT"): b_mt,
                **{("C", f"E{n}"): c_e(n) for n in range(14)}, **{("C", f"X{n}"): c_x(n) for n in range(6)},
                ("D", "xT"): d_do("xT", xdT[0:D, :], bD[0:D, 0:PT]),
                **{("D", f"t{t}"): d_do(f"t{t}", hmT[:, t, :, :].rearrange("k c t -> k (c t)"), bD[:, :]) for t in range(NT)},
                ("D", "oneT"): d_do("oneT", ohT, bD[0:EXPERTS, 0:PT])})

        @block.tensor
        def _(pe):
            def mm(dst, lhsT, rhs, start, stop):
                return pe.matmul(dst, lhsT, rhs, start=start, stop=stop, skip_group_check=True)

            resize = cs("resize")[0:IMG, :]
            pe.wait_ge(ld_w, 64)
            pe.wait_ge(ld_img, 16)
            for b in range(NB):
                ins = mm(bank[BANK_E[0]][0:IMG, 32 * b:32 * b + 32], img[:, b, :], resize, True, True)
            ins.then_inc(tok_pe, 1)
            pe.wait_ge(tok_act, 1)
            for b in range(NB):
                ins = mm(bank[BANK_E[1]][0:32, 32 * b:32 * b + 32], z_sb[:, 32 * b:32 * b + 32], resize, True, True)
            ins.then_inc(tok_pe, 1)
            pe.wait_ge(tok_act, 3)
            for g in range(2):
                for b in range(8):
                    ins = mm(bank[BANK_E[g]][0:64, D * b:D * b + D],
                             feat[:, 8 * g + b, :, :].rearrange("m i j -> m (i j)"), wt("tok")[0:8, :], True, True)
                ins.then_inc(tok_pe, 1)
            pe.wait_ge(set_vec, SET_VEC)
            pe.wait_ge(set_pool, 2)
            pe.wait_ge(set_act, 1)

            bA, bD, bO, bS = bank[BANK_A], bank[BANK_D], bank[BANK_O], bank[BANK_S]

            def transposes(dst, srcs, eye, done):
                at = 0
                for s in srcs:
                    rows, cols = s.shape[0], 1
                    for x in s.shape[1:]:
                        cols *= x
                    ins = pe.transpose(dst[0:cols, at:at + rows], s, eye)
                    at += rows
                ins.then_inc(done, 1)

            def a_xt(src, wait, name):
                def f(p):
                    wait_apart(pe, a_vec, after(A_VEC, p, wait))
                    transposes(bA, [src[:, t, 0:D] for t in range(NT)], ident, a_pe)
                return f

            def cols(b):
                return slice(P * b, P * b + P), slice(2 * P + HALF * b, 2 * P + HALF * b + HALF)

            def a_s01(p):
                pe.wait_ge(a_act, after(A_ACT, p, "xT1"))
                for b in range(2):
                    c0, c1 = cols(b)
                    mm(bA[:, T * b:T * b + P], xaT[:, c0], xaT[:, c0], True, True)
                    ins = mm(bA[:, T * b + P:T * b + T], xaT[:, c0], xaT[:, c1], True, True)
                ins.then_inc(a_pe, 1)

            def a_s2(p):
                wait_apart(pe, a_act, after(A_ACT, p, "p01"))
                for b in range(2):
                    c0, c1 = cols(b)
                    q = slice(64 * b, 64 * b + 64)
                    mm(bA[q, 0:P], xaT[:, c1], xaT[:, c0], True, True)
                    ins = mm(bA[q, P:T], xaT[:, c1], xaT[:, c1], True, True)
                ins.then_inc(a_pe, 1)

            def a_ctx(p):
                pe.wait_ge(a_act, after(A_ACT, p, "p2"))
                w = D + 1
                for b in range(2):
                    mm(bA[:, w * b:w * b + w], pA01[:, b, 0:P], xa[:, b, :], True, False)
                    mm(bA[:, w * b:w * b + w], pA2[:, 0:P], xpad[:, b, :], False, True)
                for b in range(2):
                    q = slice(64 * b, 64 * b + 64)
                    mm(bA[q, 2 * w:3 * w], pA01[:, b, P:T], xa[:, b, :], True, False)
                    ins = mm(bA[q, 2 * w:3 * w], pA2[:, P:T], xpad[:, b, :], False, True)
                ins.then_inc(a_pe, 1)

            def a_route(p):
                pe.wait_ge(a_act, after(A_ACT, p, "xT2"))
                for b in range(2):
                    c0, c1 = cols(b)
                    mm(bA[:, T * b:T * b + P], wt("wr")[0:D, :], xfT[:, c0], True, True)
                    ins = mm(bA[:, T * b + P:T * b + T], wt("wr")[0:D, :], xfT[:, c1], True, True)
                ins.then_inc(a_pe, 1)

            def a_h1(c):
                def f(p):
                    pe.wait_ge(a_act, after(A_ACT, p, ["route", "h1a"][c]))
                    mm(bA[:, 0:PT], wt("w1")[0:D, P * c:P * c + P], xfT[:, :], True, True).then_inc(a_pe, 1)
                return f

            def a_y(p):
                pe.wait_ge(a_act, after(A_ACT, p, "h1b"))
                w2 = wt("w2").rearrange("k (c d) -> k c d", c=2)
                for t in range(NT):
                    for c in range(2):
                        ins = mm(bA[:, D * t:D * t + D], h1T[:, c, P * t:P * t + P], w2[:, c, :], c == 0, c == 1)
                ins.then_inc(a_pe, 1)

            def unit(p, name):
                pe.wait_ge(ring_act, after(RING_Q, p, name))
                return bank[BANK_Q[RING_Q.index(name) % 2]]

            def b_xt(p):
                pe.wait_ge(b_vec, after(B_VEC, p, "xs"))
                transposes(unit(p, "xT")[:, :].bitcast(F32R), [xs[:, t, :] for t in range(NT)], ident_r[:, :], ring_pe)

            def b_q(t, k):
                def f(p):
                    b = unit(p, f"q{t}{k}")
                    if t == 0 and k == 0:
                        pe.wait_ge(ring_act, after(RING_Q, p, "xT") + 2)
                    mm(b[:, :], xsT[:, P * t:P * t + P], wq_hi[:, 512 * k:512 * k + 512], True, False)
                    mm(b[:, :], xsT[:, P * t:P * t + P], wq_lo[:, 512 * k:512 * k + 512], False, True).then_inc(ring_pe, 1)
                return f

            def b_kv(p):
                b = unit(p, "kv")
                for t in range(NT):
                    mm(b[:, P * t:P * t + P], xsT[:, P * t:P * t + P], wq_hi[:, 1024:1152], True, False)
                    ins = mm(b[:, P * t:P * t + P], xsT[:, P * t:P * t + P], wq_lo[:, 1024:1152], False, True)
                ins.then_inc(ring_pe, 1)

            def b_kt(k):
                def f(p):
                    b = unit(p, ["kTh", "kTl"][k])
                    if k == 0:
                        pe.wait_ge(b_vec, after(B_VEC, p, "klo"))
                    transposes(b[:, :].bitcast(F32R), [ks[:, k, t, :, :].rearrange("q c d -> q (c d)") for t in range(NT)],
                               ident_r[:, :], ring_pe)
                return f

            def b_tq(t, i):
                def f(p):
                    b = unit(p, f"tq{t}{i}")
                    if i == 0:
                        pe.wait_ge(b_pool, after(B_POOL, p, f"lo{t}"))
                    transposes(b[:, :].bitcast(F32R), [qs[:, 4 * i + j, :] for j in range(4)], ident_r[:, :], ring_pe)
                return f

            def b_s(n):
                def f(p):
                    u = p.par
                    if n == 0:
                        pe.wait_ge(b_act, p.n * len(B_ACT))
                    pe.wait_ge(s_vec, p.n * 16 + n)
                    if n < 8:
                        t, i = n // 4, n % 4
                        if n == 0:
                            pe.wait_ge(ring_act, after(RING_Q, p, "kTh") + 2)
                        mm(bS[:, :], ident_b[:, :], mask01[:, :].unsqueeze(1).broadcast_to([P, 4, P]), True, False)
                        for j in range(4):
                            ins = mm(bS[:, P * j:P * j + P], qT[u][:, t, 4 * i + j, :], kh[u][:, t, 0:P], False, j == 3)
                    else:
                        b, i = (n - 8) // 4, n % 4
                        pe.wait_ge(ring_act, after(RING_Q, p, f"tq2{i}") + 2)
                        mm(bS[:, 0:2 * T], ident_b[:, :], mask2[:, :].unsqueeze(1).broadcast_to([P, 2, T]), True, False)
                        for j in range(2):
                            h = 4 * i + 2 * j
                            ins = mm(bS[:, T * j:T * j + T], qT2[u][:, b, h:h + 2, :].rearrange("k h t -> k (h t)"), kh[u][:, b, :],
                                     False, j == 1)
                    ins.then_inc(s_pe, 1)
                return f

            def b_mt(p):
                wait_apart(pe, s_vec, p.n * 16 + 16)
                transposes(bS, [negm[:, :]], ident, mt_pe)

            def c_e(n):
                def f(p):
                    u = p.par
                    if n == 0:
                        pe.wait_ge(m_row[u], p.half * (16 * M_DMAS) + 16 * M_DMAS)
                    pe.wait_ge(e_act, p.n * 14 + n + 1)
                    b = bank[BANK_E[n % 2]][:, :]
                    if n < 8:
                        s, h = n // 4, slice(4 * (n % 4), 4 * (n % 4) + 4)
                        parts = [(sh_l01[:, :], sh_r01[:, s, h, :]), (kh[u][:, s, 0:P], qT[u][:, s, h, :]),
                                 (kl[u][:, s, :], qT[u][:, s, h, :])]
                    else:
                        h = slice(8 * (n % 2), 8 * (n % 2) + 8)
                        q = [qT2[u][:, s, h, :] for s in range(2)]
                        if n < 12:
                            s = (n - 8) // 2
                            parts = [(sh_l21[:, :], sh_r21[:, s, h, :]), (kh[u][:, s, 0:P], q[s]), (kl[u][:, s, :], q[s])]
                        else:
                            parts = [(sh_l22[:, :], sh_r22[:, h, :])] \
                                + [(kp[u][:, k, s, :], q[s]) for s in range(2) for k in range(2)]
                    for i, (lhs, rhs) in enumerate(parts):
                        ins = mm(b, lhs, rhs, i == 0, i == len(parts) - 1)
                    ins.then_inc(e_pe, 1)
                return f

            def c_v(v):
                def f(p):
                    u = p.par
                    w = D + 1
                    if v in (0, 4, 8, 10):
                        pe.wait_ge(x_act, p.n * 6 + {0: 0, 4: 2, 8: 4, 10: 5}[v])
                    else:
                        pe.wait_ge(o_vec, p.n * 12 + v)
                    if v < 8:
                        pe.wait_ge(e_act, p.n * 14 + v + 3)
                        for j in range(4):
                            ins = mm(bO[:, w * j:w * j + w], p01[:, v % 3, j, :], vx[u][:, v // 4, :], True, True)
                    else:
                        s, g = (v - 8) // 2, v % 2
                        if v < 10:
                            pe.wait_ge(e_act, p.n * 14 + v + 7)
                        for j in range(4):
                            h = 8 * g + 2 * j
                            mm(bO[:, w * j:w * j + w], p21[:, s, h:h + 2, :].rearrange("s h t -> s (h t)"), vx[u][:, s, :], True, False)
                            ins = mm(bO[:, w * j:w * j + w], p22[:, h:h + 2, :].rearrange("s h t -> s (h t)"), vp[u][:, s, :], False, True)
                    ins.then_inc(o_pe, 1)
                return f

            def c_x(n):
                def f(p):
                    if n in (0, 2, 4, 5):
                        pe.wait_ge(o_vec, p.n * 12 + {0: 4, 2: 8, 4: 10, 5: 12}[n])
                    else:
                        pe.wait_ge(x_act, p.n * 6 + n)
                    srcs = [on[:, 8 * (n % 2) + 2 * j:8 * (n % 2) + 2 * j + 2, :] for j in range(4)]
                    transposes(bO, [s.rearrange("q h d -> q (h d)") for s in srcs], ident, x_pe)
                return f

            wo01 = wt("wo01").rearrange("k (j d) -> k j d", j=8)
            wo2 = wt("wo2").rearrange("k (j g d) -> k j g d", j=4, g=2)

            def c_wo(t):
                def f(p):
                    pe.wait_ge(x_act, p.n * 6 + 2 * t + 2)
                    if t == 0:
                        pe.wait_ge(d_vec, p.n * len(D_VEC))
                    if t < 2:
                        for j in range(8):
                            ins = mm(bD[:, D * t:D * t + D], oT[:, j, :], wo01[:, j, :], j == 0, j == 7)
                    else:
                        for b in range(2):
                            q = slice(64 * b, 64 * b + 64)
                            for j in range(4):
                                for g in range(2):
                                    ins = mm(bD[q, 2 * D:3 * D], oT[:, 4 * b + j, 64 * g:64 * g + 64], wo2[:, j, g, :],
                                             j + g == 0, j + g == 4)
                    ins.then_inc(d_pe, 1)
                return f

            def d_xt(p):
                wait_apart(pe, d_vec, after(D_VEC, p, "xn"))
                transposes(bD, tiles(xd), ident, d_pe)

            def d_logits(p):
                pe.wait_ge(d_act, after(D_ACT, p, "xT"))
                for t in range(NT):
                    ins = mm(bD[:, EXPERTS * t:EXPERTS * t + EXPERTS], xdT[:, P * t:P * t + P], wt("rout")[0:D + 1, :], True, True)
                ins.then_inc(d_pe, 1)

            def d_h(t):
                def f(p):
                    pe.wait_ge(d_vec, after(D_VEC, p, ["logits", "hm0", "hm1"][t]))
                    mm(bD[:, :], xdT[:, P * t:P * t + P], wt("e1")[0:D + 1, :], True, True).then_inc(d_pe, 1)
                return f

            def d_t(t):
                def f(p):
                    if t == 0:
                        pe.wait_ge(d_vec, after(D_VEC, p, "hm2"))
                    else:
                        pe.wait_ge(d_act, after(D_ACT, p, f"t{t - 1}"))
                    transposes(bD, [hm[:, t, P * c:P * c + P] for c in range(4)], ident, d_pe)
                return f

            def d_onet(p):
                pe.wait_ge(d_act, after(D_ACT, p, "t2"))
                transposes(bD, tiles(one_hot), ident, d_pe)

            def d_out(p):
                pe.wait_ge(d_act, after(D_ACT, p, "oneT"))
                e2 = wt("e2").rearrange("k (c d) -> k c d", c=4)
                for t in range(NT):
                    dst = bD[:, D * t:D * t + D]
                    mm(dst, ohT[:, P * t:P * t + P], wt("e2b")[0:EXPERTS, :], True, False)
                    for c in range(4):
                        ins = mm(dst, hmT[:, t, c, :], e2[:, c, :], False, c == 3)
                ins.then_inc(d_pe, 1)

            run_program(pe, {
                ("A", "xT1"): a_xt(xa, "xn1", "xT1"), ("A", "s01"): a_s01, ("A", "s2"): a_s2, ("A", "ctx"): a_ctx,
                ("A", "xT2"): a_xt(xf, "xn2", "xT2"), ("A", "route"): a_route, ("A", "h1a"): a_h1(0), ("A", "h1b"): a_h1(1),
                ("A", "y"): a_y, ("B", "xT"): b_xt, **{("B", f"q{t}{k}"): b_q(t, k) for t in range(NT) for k in range(2)},
                ("B", "kv"): b_kv, ("B", "kTh"): b_kt(0), ("B", "kTl"): b_kt(1),
                **{("B", f"tq{t}{i}"): b_tq(t, i) for t in range(NT) for i in range(4)},
                **{("B", f"S{n}"): b_s(n) for n in range(16)}, ("B", "mT"): b_mt,
                **{("C", f"E{n}"): c_e(n) for n in range(14)}, **{("C", f"V{v}"): c_v(v) for v in range(12)},
                **{("C", f"X{n}"): c_x(n) for n in range(6)},
                **{("C", f"wo{t}"): c_wo(t) for t in range(NT)}, ("D", "xT"): d_xt, ("D", "logits"): d_logits,
                **{("D", f"h{t}"): d_h(t) for t in range(NT)}, **{("D", f"t{t}"): d_t(t) for t in range(NT)},
                ("D", "oneT"): d_onet, ("D", "out"): d_out})


def haar_resize():
    import numpy as np

    def haar(n, sign):
        m = np.zeros((n // 2, n))
        for i in range(n // 2):
            m[i, 2 * i], m[i, 2 * i + 1] = 1.0, sign
        return m * 0.7071067811865476

    def resize(n):
        scale = n / 8
        at = (np.arange(8) + 0.5) * scale - 0.5
        w = np.maximum(0.0, 1.0 - np.abs(at[None, :] - np.arange(n)[:, None]) / scale)
        return (w / w.sum(0, keepdims=True)).T

    lo1 = haar(IMG, 1.0)
    ops = [resize(IMG // 4) @ haar(IMG // 2, 1.0) @ lo1, resize(IMG // 4) @ haar(IMG // 2, -1.0) @ lo1,
           resize(IMG // 2) @ lo1, resize(IMG // 2) @ haar(IMG, -1.0)]
    return np.concatenate(ops, 0).T


def shape_constants():
    import numpy as np

    row, s, t64 = np.arange(P), np.arange(P), np.arange(HALF)
    c = {"ident": np.eye(P)}
    c["mask01"] = np.where(s[None, :] > row[:, None], NEG, 0.0)
    t2, s2 = P + row[:, None] % HALF, np.arange(T)[None, :]
    c["mask2"] = np.where((s2 > t2) | (t2 - s2 > WINDOW), NEG, 0.0)
    c["b01"] = np.where(row[:, None] > s[None, :], NEG, 0.0)
    c["b21"] = np.where(row[:, None] < P + t64[None, :] - WINDOW, NEG, 0.0)
    c["b22"] = np.where(row[:, None] % HALF > t64[None, :], NEG, 0.0)
    for name, free in (("a01", [(0, 0, P)]), ("a21", [(P - 1, 0, P)]), ("a22", [(0, 0, HALF), (HALF, HALF, P)])):
        a = np.eye(P)
        for r, lo, hi in free:
            a[r, lo:hi] = 1.0
        c[name] = a
    freqs = np.float32(10000.0) ** (np.float32(-2.0) * np.arange(D // 2, dtype=np.float32) / np.float32(D))
    pos = np.stack([row, row, P + row % HALF], 1).astype(np.float32)
    theta = (pos[:, :, None] * freqs[None, None, :]).astype(np.float32)
    c["rope"] = np.concatenate([np.cos(theta), np.sin(theta)], 2).reshape(P, NT * D)
    c["iota"] = np.tile(np.arange(EXPERTS), (P, 1))
    j = np.arange(T)[None, None, :]
    own = np.stack([row, P + row % HALF], 1)[:, :, None]
    c["before"] = (j < own).reshape(P, 2 * T)
    c["resize"] = np.concatenate([haar_resize(), np.zeros((P - IMG, 32))], 0)
    return [np.ascontiguousarray(np.concatenate([c[n].astype(np.float32) for n in cols], 1)) for cols in (SHAPE_COLS, MASK_COLS)]


def packed_weights(i):
    import numpy as np

    def rows(a):
        a = np.asarray(a)
        return np.concatenate([a, np.zeros((P - a.shape[0], a.shape[1]), a.dtype)], 0)

    w = {n: np.asarray(a) for n, a in i.items()}
    wo = w["L1_attn_wo"].T.reshape(NH, D, D)
    c = {}
    c["wo01"] = wo.reshape(8, P, D).transpose(1, 0, 2).reshape(P, 512)
    c["wo2"] = wo.reshape(4, 2, 2, D, D).transpose(1, 3, 0, 2, 4).reshape(P, 512)
    c["w1"] = rows(w["L0_ffn_w1"])
    c["w2"] = w["L0_ffn_w2"].reshape(2, P, D).transpose(1, 0, 2).reshape(P, 2 * D)
    c["wr"] = rows(np.repeat(w["L0_ffn_wr"], P, 1))
    c["br"] = np.repeat(w["L0_ffn_br"].reshape(1, 1), P, 0)
    c["b1"] = w["L0_ffn_b1"].reshape(2, P).T
    for n, k in (("b2", "L0_ffn_b2"), ("qn", "L1_attn_q_norm_w"), ("kn", "L1_attn_k_norm_w")):
        c[n] = np.repeat(w[k].reshape(1, D), P, 0)
    c["rout"] = rows(np.concatenate([w["L1_ffn_router_w"].T, w["L1_ffn_router_b"].reshape(1, -1)], 0))
    c["e1"] = rows(np.concatenate([w["L1_ffn_W1"].transpose(1, 0, 2).reshape(D, -1), w["L1_ffn_b1"].reshape(1, -1)], 0))
    c["e2"] = w["L1_ffn_W2"].reshape(4, P, D).transpose(1, 0, 2).reshape(P, 4 * D)
    c["e2b"] = rows(w["L1_ffn_b2"])
    c["tok"] = rows(np.concatenate([w["L0_tok_W"], w["L0_tok_b"].reshape(1, -1)], 0))
    return np.ascontiguousarray(np.concatenate([c[n] for n in WEIGHT_COLS], 1))


def kernel(**inputs):
    import numpy as np
    from concourse import bacc
    from concourse.bass_utils import run_bass_kernel_spmd

    nc = bacc.Bacc("TRN2", target_bir_lowering=False, num_devices=1)
    shapes, masks = shape_constants()
    wqkv = np.concatenate([np.asarray(inputs["L1_attn_wq"]), np.asarray(inputs["L1_attn_wkv"])], 0).T
    arrays = {
        "shapes": shapes,
        "masks": masks,
        "weights": packed_weights({n: a for n, a in inputs.items() if n not in ("x", "txt", "L0_ffn_attention_mask")}),
        "wqkv": np.ascontiguousarray(np.concatenate([wqkv, wqkv], 0)),
        "images": np.ascontiguousarray(np.asarray(inputs["x"])[:, 0].transpose(1, 0, 2)),
        "txt": np.ascontiguousarray(inputs["txt"]),
    }
    aps = [nc.dram_tensor(n, a.shape, F32, kind="ExternalInput").ap() for n, a in arrays.items()]
    out = nc.dram_tensor("out", (NB, T, D), F32, kind="ExternalOutput").ap()
    early_fusion(nc, *aps, out)
    r = run_bass_kernel_spmd(nc, [arrays], core_ids=[0])
    return r.results[0]["out"]
```
